# Optimizing a Trainium2 kernel written in Bass

```python
import numpy as np
import jax
import jax.numpy as jnp

def _softmax(x, axis=-1):
    return jax.nn.softmax(x, axis=axis)
def _gelu(x):
    return jax.nn.gelu(x, approximate=True)
def _silu(x):
    return jax.nn.silu(x)
def _sigmoid(x):
    return jax.nn.sigmoid(x)
def _layernorm(x, axis=-1, eps=1e-5):
    m = jnp.mean(x, axis=axis, keepdims=True)
    v = jnp.var(x, axis=axis, keepdims=True)
    return (x - m) / jnp.sqrt(v + eps)
def _scatter_add(tgt, idx, src, axis=0):
    return tgt.at[idx].add(src)
def _segment_sum(src, seg, n):
    return jax.ops.segment_sum(src, seg, n)

kernel_name = 'mk_conv_preact_d1_conv_nchw512_a931c7'

def setup_inputs(seed: int = 0):
    np.random.seed(seed)
    _w = jnp.asarray
    def _rec_inputs():
        import jax
        import jax.numpy as jnp
        _gk = jax.random.key(seed)
        x = -7.109e-05 + 0.9999 * jax.random.normal(jax.random.fold_in(_gk, 1), (8, 512, 128, 128), jnp.float32)
        return x
    x = _rec_inputs()
    def _L0_conv_setup():
        import jax, jax.numpy as jnp
        import numpy as np
        GROUPS = 32
        C = 512
        CG = C // GROUPS
        B, H, W = (8, 128, 128)
        EPS = 1e-05

        def _gn(x, w, b):
            m = jnp.mean(x, axis=(2, 3), keepdims=True)
            v = jnp.mean((x - m) ** 2, axis=(2, 3), keepdims=True)
            xn = (x - m) * jax.lax.rsqrt(v + EPS)
            return xn * w[None, :, None, None] + b[None, :, None, None]

        def _conv1x1(x, w, b):
            return jnp.einsum('nchw,oc->nohw', x, w) + b[None, :, None, None]
        key = jax.random.key(seed)
        ks = jax.random.split(key, 12)
        s = lambda k, shape: jax.random.normal(k, shape, dtype=jnp.float32) * 0.05
        return {'x': jax.random.normal(ks[0], (B, C, H, W), dtype=jnp.float32), 'w_cc': s(ks[1], (CG, 2 * CG)), 'b_cc': s(ks[2], (CG,)), 'gn1_w': jnp.ones((CG,), jnp.float32), 'gn1_b': jnp.zeros((CG,), jnp.float32), 'w_s1': s(ks[3], (CG, CG)), 'b_s1': s(ks[4], (CG,)), 'w_ph': s(ks[5], (CG, CG)), 'b_ph': s(ks[6], (CG,)), 'w_pw': s(ks[7], (CG, CG)), 'b_pw': s(ks[8], (CG,)), 'w_s3': s(ks[9], (CG, CG, 3, 3)), 'b_s3': s(ks[10], (CG,)), 'gn2_w': jnp.ones((CG,), jnp.float32), 'gn2_b': jnp.zeros((CG,), jnp.float32)}
    _L0_conv_all = _L0_conv_setup()
    _L0_conv_in = {k: v for k, v in _L0_conv_all.items() if k in ('w_cc', 'b_cc', 'gn1_w', 'gn1_b', 'w_s1', 'b_s1', 'w_ph', 'b_ph', 'w_pw', 'b_pw', 'w_s3', 'b_s3', 'gn2_w', 'gn2_b', )}
    del _L0_conv_all

    return {
        "x": x,
        "L0_conv_w_cc": _L0_conv_in["w_cc"],
        "L0_conv_b_cc": _L0_conv_in["b_cc"],
        "L0_conv_gn1_w": _L0_conv_in["gn1_w"],
        "L0_conv_gn1_b": _L0_conv_in["gn1_b"],
        "L0_conv_w_s1": _L0_conv_in["w_s1"],
        "L0_conv_b_s1": _L0_conv_in["b_s1"],
        "L0_conv_w_ph": _L0_conv_in["w_ph"],
        "L0_conv_b_ph": _L0_conv_in["b_ph"],
        "L0_conv_w_pw": _L0_conv_in["w_pw"],
        "L0_conv_b_pw": _L0_conv_in["b_pw"],
        "L0_conv_w_s3": _L0_conv_in["w_s3"],
        "L0_conv_b_s3": _L0_conv_in["b_s3"],
        "L0_conv_gn2_w": _L0_conv_in["gn2_w"],
        "L0_conv_gn2_b": _L0_conv_in["gn2_b"],
    }

def reference(x, L0_conv_w_cc, L0_conv_b_cc, L0_conv_gn1_w, L0_conv_gn1_b, L0_conv_w_s1, L0_conv_b_s1, L0_conv_w_ph, L0_conv_b_ph, L0_conv_w_pw, L0_conv_b_pw, L0_conv_w_s3, L0_conv_b_s3, L0_conv_gn2_w, L0_conv_gn2_b):
    import jax
    import jax.numpy as jnp
    def _L0_conv_ref(x, w_cc, b_cc, gn1_w, gn1_b, w_s1, b_s1, w_ph, b_ph, w_pw, b_pw, w_s3, b_s3, gn2_w, gn2_b):
        import jax, jax.numpy as jnp
        import numpy as np
        GROUPS = 32
        C = 512
        CG = C // GROUPS
        B, H, W = (8, 128, 128)
        EPS = 1e-05

        def _gn(x, w, b):
            m = jnp.mean(x, axis=(2, 3), keepdims=True)
            v = jnp.mean((x - m) ** 2, axis=(2, 3), keepdims=True)
            xn = (x - m) * jax.lax.rsqrt(v + EPS)
            return xn * w[None, :, None, None] + b[None, :, None, None]

        def _conv1x1(x, w, b):
            return jnp.einsum('nchw,oc->nohw', x, w) + b[None, :, None, None]
        b, c, h, w = x.shape
        gx = x.reshape(b * GROUPS, c // GROUPS, h, w)
        gap = jnp.mean(gx, axis=(2, 3), keepdims=True)
        gmp = jnp.max(gx, axis=(2, 3), keepdims=True)
        ch = _conv1x1(jnp.concatenate([gap, gmp], axis=1), w_cc, b_cc)
        channel_weight = jax.nn.sigmoid(_gn(ch, gn1_w, gn1_b))
        x_h = jnp.mean(gx, axis=3, keepdims=True)
        x_w = jnp.mean(gx, axis=2, keepdims=True).transpose(0, 1, 3, 2)
        hw = _conv1x1(jnp.concatenate([x_h, x_w], axis=2), w_s1, b_s1)
        xh, xw = (hw[:, :, :h], hw[:, :, h:])
        pos_h = jax.nn.sigmoid(_conv1x1(xh, w_ph, b_ph))
        pos_w = jax.nn.sigmoid(_conv1x1(xw.transpose(0, 1, 3, 2), w_pw, b_pw))
        sx = gx * pos_h * pos_w
        sx = jax.lax.conv_general_dilated(sx, w_s3, (1, 1), 'SAME', dimension_numbers=('NCHW', 'OIHW', 'NCHW')) + b_s3[None, :, None, None]
        spatial_weight = jax.nn.sigmoid(_gn(sx, gn2_w, gn2_b))
        out = gx * (channel_weight * spatial_weight)
        return out.reshape(b, c, h, w)

    def _gn(v, G=32, eps=1e-5):
        B_, C_, H_, W_ = v.shape
        g = v.reshape(B_, G, C_ // G, H_, W_)
        m = jnp.mean(g, axis=(2, 3, 4), keepdims=True)
        s = jnp.var(g, axis=(2, 3, 4), keepdims=True)
        return ((g - m) / jnp.sqrt(s + eps)).reshape(v.shape)

    def _ln_c(v, eps=1e-6):
        m = jnp.mean(v, axis=1, keepdims=True)
        s = jnp.var(v, axis=1, keepdims=True)
        return (v - m) / jnp.sqrt(s + eps)

    def _ln_t(v, eps=1e-5):
        m = jnp.mean(v, axis=-1, keepdims=True)
        s = jnp.var(v, axis=-1, keepdims=True)
        return (v - m) / jnp.sqrt(s + eps)

    def _to_tokens(v):
        B_, C_, H_, W_ = v.shape
        return v.reshape(B_, C_, H_ * W_).transpose(0, 2, 1)
    def _from_tokens(t, like):
        B_, C_, H_, W_ = like.shape
        return t.transpose(0, 2, 1).reshape(B_, C_, H_, W_)

    x = x + _L0_conv_ref(_gn(x), L0_conv_w_cc, L0_conv_b_cc, L0_conv_gn1_w, L0_conv_gn1_b, L0_conv_w_s1, L0_conv_b_s1, L0_conv_w_ph, L0_conv_b_ph, L0_conv_w_pw, L0_conv_b_pw, L0_conv_w_s3, L0_conv_b_s3, L0_conv_gn2_w, L0_conv_gn2_b)
    return x


_drawn_inputs = setup_inputs


def setup_inputs(seed=0):
    import zlib

    import numpy as np

    out = dict(_drawn_inputs(seed))
    spreads = {'L0_conv_gn1_w': (1.0, 0.2),
     'L0_conv_gn1_b': (0.0, 0.8),
     'L0_conv_gn2_w': (1.0, 0.6),
     'L0_conv_gn2_b': (0.0, 0.8)}
    factors = {'L0_conv_w_s1': 22.983,
     'L0_conv_b_s1': 8.0,
     'L0_conv_w_ph': 8.0,
     'L0_conv_b_ph': 8.0,
     'L0_conv_w_pw': 8.0,
     'L0_conv_b_pw': 8.0,
     'L0_conv_b_s3': 64.0}
    for name, (base, spread) in spreads.items():
        noise = np.random.default_rng([zlib.crc32(name.encode()), seed]).standard_normal(out[name].shape)
        drawn = base * np.exp(spread * noise) if base else spread * noise
        out[name] = jnp.asarray(drawn.astype(out[name].dtype))
    for name, factor in factors.items():
        out[name] = (out[name] * factor).astype(out[name].dtype)
    return out
```

```python
from contextlib import ExitStack

import concourse.bass as bass
from concourse import mybir

F32 = mybir.dt.float32
BF16 = mybir.dt.bfloat16
ALU = mybir.AluOpType
ACT = mybir.ActivationFunctionType
AX_X = mybir.AxisListType.X

P = 128
N, C, HT, W = 8, 512, 128, 128
CG = 16
RB = P // CG
NB = HT // RB
GROUPS = N * C // CG
PIX = HT * W
WP = W + 2
UNITS = GROUPS // 2
XS = 4
EPS = 1e-5
KW = 3
HALO = 2 * CG * KW
HALF = 2
BB = 4
RUN = (NB - 2) * WP + W
ACT_BANDS = 13
PER = 4


def conv_attention(nc, x, wcc, wconv, ws1, wph, wpw, vecs, same_channel, row_masks, halo_mask, out):
    x_g = x.rearrange("n (g c) (b r) w -> (n g) r c b w", c=CG, r=RB)
    out_g = out.rearrange("n (g c) (b r) w -> (n g) r c b w", c=CG, r=RB)

    with ExitStack() as ctx:
        def sb(name, shape, dt=F32):
            return ctx.enter_context(nc.sbuf_tensor(name, shape, dt))

        def psum(name, shape):
            return ctx.enter_context(nc.psum_tensor(name, shape, F32))

        def sem(name):
            return ctx.enter_context(nc.semaphore(name))

        xt = sb("xt", [P, XS, 2, NB, W])
        gated = sb("gated", [P, 2, 2, NB, WP])
        halo = sb("halo", [HALO, 2, 2, NB * WP])
        sp_buf = sb("sp_buf", [P, 4, NB, W])
        junk = sb("junk", [P, 3, NB * W], BF16)
        wcc_rep = sb("wcc_rep", [P, 2, CG])
        wconv_rep = sb("wconv_rep", [P, KW, 3, CG])
        whalo_in = sb("whalo_in", [HALO, CG])
        ws1_rep = sb("ws1_rep", [P, CG])
        wph_rep = sb("wph_rep", [P, CG])
        wpw_rep = sb("wpw_rep", [P, CG])
        masks = sb("masks", [P, 3, RB])
        hmask = sb("hmask", [HALO, RB])
        vec = sb("vec", [P, 9])
        W_conv = sb("W_conv", [P, KW, P])
        w_part = sb("w_part", [P, 2, KW, P])
        W_halo = sb("W_halo", [HALO, P])
        W_s1h = sb("W_s1h", [P, P])
        W_s1w = sb("W_s1w", [P, P])
        W_rows = sb("W_rows", [P, P])
        W_cols = sb("W_cols", [P, P])
        b_pos = sb("b_pos", [P, 2])
        W_ph = sb("W_ph", [P, P])
        W_pw = sb("W_pw", [P, P])
        W_gap = sb("W_gap", [P, P])
        W_gmp = sb("W_gmp", [P, P])
        M_all = sb("M_all", [P, P])
        M_chan = sb("M_chan", [P, P])
        S_chan = sb("S_chan", [P, P])
        sums = sb("sums", [P, 2, 2, NB + W])
        sums_n = sb("sums_n", [P, 2, 2, NB + W])
        tot = sb("tot", [P, 2, 2])
        mx = sb("mx", [P, 2, 2])
        mx_x = sb("mx_x", [P, 2, 2, RB])
        gmx = sb("gmx", [P, 2, 2])
        gap_n = sb("gap_n", [P, 2, 2])
        gmx_n = sb("gmx_n", [P, 2, 2])
        gap_s = sb("gap_s", [P, 2, 2])
        negm = sb("negm", [P, 4, 2])
        ssq = sb("ssq", [P, 2, 2])
        var_e = sb("var_e", [P, 2, 2])
        rstd = sb("rstd", [P, 4, 2])
        gate_h = sb("gate_h", [P, 2, 2, NB])
        gate_hr = sb("gate_hr", [P, 2, 2, NB])
        gate_w = sb("gate_w", [P, 2, 2, W])
        ch = sb("ch", [P, 10, 2])
        cgate = sb("cgate", [P, 2, 2])
        kfac = sb("kfac", [P, 4, 2])
        consts = sb("consts", [P, 8])
        ssum2 = sb("ssum2", [P, 4, 2])
        share2 = sb("share2", [P, 4, 2])
        negm2 = sb("negm2", [P, 4])
        ssq2 = sb("ssq2", [P, 4])
        var2_e = sb("var2_e", [P, 4])
        rstd2 = sb("rstd2", [P, 4])
        scale2 = sb("scale2", [P, 4])
        sh2 = sb("sh2", [P, 4])
        bias2 = sb("bias2", [P, 4])

        conv_ps = psum("conv_ps", [P, 2, HALF * BB, W])
        norm_ps = psum("norm_ps", [P, 512])
        pos_ps = psum("pos_ps", [P, 512])
        gn2_ps = psum("gn2_ps", [P, 512])
        cw_ps = psum("cw_ps", [P, 512])

        w_in = sem("w_in")
        w_dve = sem("w_dve")
        w_pe = sem("w_pe")
        w_pool = sem("w_pool")
        x_in = [[sem(f"x_in{s}{j}") for j in range(2)] for s in range(XS)]
        halo_in = [[sem(f"halo_in{s}{j}") for j in range(2)] for s in range(2)]
        stored = [sem(f"stored{s}") for s in range(4)]
        sums_done = sem("sums_done")
        tot_done = sem("tot_done")
        mx_done = sem("mx_done")
        mxx_done = sem("mxx_done")
        mean_mm = sem("mean_mm")
        negm_done = sem("negm_done")
        sq_done = sem("sq_done")
        var_mm = sem("var_mm")
        var_done = sem("var_done")
        rstd_done = sem("rstd_done")
        sn_done = sem("sn_done")
        pos_mm = sem("pos_mm")
        gates_done = sem("gates_done")
        ghr_done = sem("ghr_done")
        gp_act = sem("gp_act")
        gp_dve = sem("gp_dve")
        mod_done = sem("mod_done")
        conv_mm = sem("conv_mm")
        evac = sem("evac")
        mean2_mm = sem("mean2_mm")
        negm2_done = sem("negm2_done")
        sq2_done = sem("sq2_done")
        var2_mm = sem("var2_mm")
        var2_done = sem("var2_done")
        aff2 = sem("aff2")
        sig2 = sem("sig2")
        fin_a = sem("fin_a")
        final = sem("final")
        mxs_mm = sem("mxs_mm")
        gmx_done = sem("gmx_done")
        cin = sem("cin")
        ch_mm = sem("ch_mm")
        ch_done = sem("ch_done")
        cgn = sem("cgn")
        cgate_done = sem("cgate_done")
        kfac_done = sem("kfac_done")

        def later(n, first):
            return not isinstance(n, int) or n >= first

        def real(u):
            return not isinstance(u, int) or 0 <= u < UNITS

        def turns(eng, body):
            first, last = 1, (UNITS - 4) // PER
            for t in range(-3, first * PER):
                body(t, t % PER)
            with eng.Fori(first, last) as turn:
                for q in range(PER):
                    body(turn * PER + q, q)
            for t in range(last * PER, UNITS + 1):
                body(t, t % PER)

        V = {n: vec[:, i:i + 1] for i, n in enumerate(
            ("b_cc", "gn1_w", "gn1_b", "b_s1", "b_ph", "b_pw", "b_s3", "gn2_w", "gn2_b"))}

        block = ctx.enter_context(nc.Block())

        @block.sync
        def _(sp):
            rep = [(wcc_rep[:], wcc, 2 * CG), (wconv_rep[:], wconv, KW * 3 * CG), (ws1_rep[:], ws1, CG),
                   (wph_rep[:], wph, CG), (wpw_rep[:], wpw, CG)]
            n_in = 0
            for dst, src, k in rep:
                s = src.rearrange("c k -> c () k").to_broadcast([CG, RB, k])
                sp.dma_start(dst, s).then_inc(w_in, 16)
                n_in += 1
            for i, v in enumerate(vecs):
                s = v.rearrange("(c a b) -> c a b", a=1, b=1).to_broadcast([CG, RB, 1])
                sp.dma_start(vec[:, i:i + 1], s).then_inc(w_in, 16)
                n_in += 1
            hv = wconv.rearrange("c (kw kh o) -> (c kw) kh o", kw=KW, kh=3)
            sp.dma_start(whalo_in[0:HALO // 2, :], hv[:, 0, :]).then_inc(w_in, 16)
            sp.dma_start(whalo_in[HALO // 2:HALO, :], hv[:, 2, :]).then_inc(w_in, 16)
            sp.dma_start(S_chan[:, :], same_channel).then_inc(w_in, 16)
            sp.dma_start(masks[:], row_masks).then_inc(w_in, 16)
            sp.dma_start(hmask[:, :], halo_mask).then_inc(w_in, 16)

            def body(t, q):
                u, s = t - 1, (q - 1) % XS
                v, vs = t + 3, (q + 3) % XS
                h, hs = t + 1, (q + 1) % 2

                def group(rows, n):
                    size = CG * PIX
                    at = n * size if isinstance(n, int) else sp.snap(n * size)
                    first = rows[0, 0]
                    return [bass.AP(tensor=first.tensor, offset=at + r * W, ap=[list(d) for d in first.ap])
                            for r in range(RB)]

                def load(j):
                    if real(v):
                        come = group(x_g, 2 * v + j)
                        if later(v, XS):
                            sp.wait_ge(final, 2 * (v - XS) + j + 1)
                        for r in range(RB):
                            sp.dma_start(xt[r:P:RB, vs, j], come[r]).then_inc(x_in[vs][j], 16)

                def store(j):
                    if real(u):
                        g = 2 * (s % 2) + j
                        to = group(out_g, 2 * u + j)
                        sp.wait_ge(final, 2 * u + j + 1)
                        for r in range(RB):
                            sp.dma_start(to[r], sp_buf[r:P:RB, g]).then_inc(stored[g], 16)

                def halo_rows(j):
                    if real(h):
                        flat = gated[:, hs, j].rearrange("p b w -> p (b w)")
                        sp.wait_ge(mod_done, 2 * h + j + 1)
                        for side in range(2):
                            row = RB - 1 if side == 0 else 0
                            src = flat[row:P:RB, 0:NB * WP]
                            at = 0 if side == 0 else WP
                            shifts = bass.AP(tensor=src.tensor, offset=src.offset + at,
                                             ap=[list(src.ap[0]), [1, KW], [1, RUN]])
                            to = WP if side == 0 else 0
                            sp.dma_start(halo[side * CG * KW:(side + 1) * CG * KW, hs, j, to:to + RUN],
                                         shifts).then_inc(halo_in[hs][j], 16)

                load(0)
                store(0)
                halo_rows(0)
                halo_rows(1)
                load(1)
                store(1)

            turns(sp, body)
            for g in range(4):
                sp.wait_ge(stored[g], 16 * RB * (GROUPS // 4))

        @block.gpsimd
        def _(pool):
            nc.gpsimd.memset(M_all[:, :], 1.0 / (CG * PIX)).then_inc(w_pool, 1)
            for i, value in enumerate((-0.5, 1.0 / (NB * W), 1.0, EPS)):
                nc.gpsimd.memset(consts[:, 2 * i:2 * i + 2], value).then_inc(w_pool, 1)
            nc.gpsimd.memset(halo[:], 0.0).then_inc(w_pool, 1)
            pool.wait_ge(w_pool, 6)
            pool.wait_ge(w_in, 16 * 19)

            def affine2(u, s, j):
                g = 2 * (s % 2) + j
                n = 2 * u + j
                pool.wait_ge(var2_done, n + 1)
                if later(n, 4):
                    pool.wait_ge(sig2, n - 3)
                nc.gpsimd.tensor_tensor(rstd2[:, g:g + 1], var2_e[:, g:g + 1], consts[:, 0:1],
                                        ALU.pow).then_inc(aff2, 1)
                pool.wait_ge(aff2, 4 * n + 1)
                nc.gpsimd.tensor_tensor(scale2[:, g:g + 1], rstd2[:, g:g + 1], V["gn2_w"],
                                        ALU.mult).then_inc(aff2, 1)
                pool.wait_ge(aff2, 4 * n + 2)
                nc.gpsimd.tensor_tensor(sh2[:, g:g + 1], scale2[:, g:g + 1], negm2[:, g:g + 1],
                                        ALU.mult).then_inc(aff2, 1)
                pool.wait_ge(aff2, 4 * n + 3)
                nc.gpsimd.tensor_tensor(bias2[:, g:g + 1], sh2[:, g:g + 1], V["gn2_b"],
                                        ALU.add).then_inc(aff2, 1)

            def channel_in(u, s):
                d = s % 2
                pool.wait_ge(tot_done, u + 1)
                if later(u, 2):
                    pool.wait_ge(ch_mm, u - 1)
                nc.gpsimd.tensor_tensor(gap_s[:, d], tot[:, d], consts[:, 2:4], ALU.mult).then_inc(cin, 1)
                pool.wait_ge(cin, 3 * u + 1)
                pool.wait_ge(negm_done, u + 1)
                nc.gpsimd.tensor_tensor(gap_n[:, d], gap_s[:, d], negm[:, s], ALU.add).then_inc(cin, 1)
                pool.wait_ge(gmx_done, u + 1)
                nc.gpsimd.tensor_tensor(gmx_n[:, d], gmx[:, d], negm[:, s], ALU.add).then_inc(cin, 1)

            def channel_norm(u, s):
                pool.wait_ge(ch_done, u + 1)

                if later(u, 1):
                    pool.wait_ge(cgate_done, u)
                nc.gpsimd.tensor_tensor(ch[:, 1], ch[:, 0], V["b_cc"].to_broadcast([P, 2]), ALU.add).then_inc(cgn, 1)
                pool.wait_ge(cgn, 9 * u + 1)
                nc.gpsimd.tensor_tensor(ch[:, 2], ch[:, 1], consts[:, 4:6], ALU.mult).then_inc(cgn, 1)
                pool.wait_ge(cgn, 9 * u + 2)
                nc.gpsimd.tensor_tensor(ch[:, 3], ch[:, 1], ch[:, 2], ALU.subtract).then_inc(cgn, 1)
                pool.wait_ge(cgn, 9 * u + 3)
                nc.gpsimd.tensor_tensor(ch[:, 4], ch[:, 3], ch[:, 3], ALU.mult).then_inc(cgn, 1)
                pool.wait_ge(cgn, 9 * u + 4)
                nc.gpsimd.tensor_tensor(ch[:, 5], ch[:, 4], consts[:, 6:8], ALU.add).then_inc(cgn, 1)
                pool.wait_ge(cgn, 9 * u + 5)
                nc.gpsimd.tensor_tensor(ch[:, 6], ch[:, 5], consts[:, 0:2], ALU.pow).then_inc(cgn, 1)
                pool.wait_ge(cgn, 9 * u + 6)
                nc.gpsimd.tensor_tensor(ch[:, 7], ch[:, 3], ch[:, 6], ALU.mult).then_inc(cgn, 1)
                pool.wait_ge(cgn, 9 * u + 7)
                nc.gpsimd.tensor_tensor(ch[:, 8], ch[:, 7], V["gn1_w"].to_broadcast([P, 2]), ALU.mult).then_inc(cgn, 1)
                pool.wait_ge(cgn, 9 * u + 8)
                nc.gpsimd.tensor_tensor(ch[:, 9], ch[:, 8], V["gn1_b"].to_broadcast([P, 2]), ALU.add).then_inc(cgn, 1)

            def body(t, q):
                a, sa = t + 1, (q + 1) % XS
                b, sb_ = t - 1, (q - 1) % XS
                if real(a):
                    pool.wait_ge(var_done, a + 1)
                    if later(a, 4):
                        pool.wait_ge(final, 2 * (a - XS) + 2)
                    nc.gpsimd.tensor_tensor(rstd[:, sa], var_e[:, sa % 2], consts[:, 0:2],
                                            ALU.pow).then_inc(rstd_done, 1)
                if real(b):
                    affine2(b, sb_, 1)
                if real(a):
                    channel_in(a, sa)
                    channel_norm(a, sa)
                if real(t):
                    affine2(t, q, 0)
                if real(a):
                    pool.wait_ge(cgate_done, a + 1)
                    pool.wait_ge(rstd_done, a + 1)
                    nc.gpsimd.tensor_tensor(kfac[:, sa], cgate[:, sa % 2], rstd[:, sa],
                                            ALU.mult).then_inc(kfac_done, 1)

            turns(pool, body)

        @block.scalar
        def _(act):
            act.wait_ge(w_in, 16 * 19)
            act.wait_ge(w_pool, 6)

            def evacuate(u, s, h):
                j, k = h // 2, h % 2
                g = 2 * (s % 2) + j
                act.wait_ge(conv_mm, 4 * u + h + 1)
                if k == 0:
                    if later(u, 2):
                        act.wait_ge(stored[g], 8 * RB * (u - s % 2))
                nc.scalar.activation(sp_buf[:, g, k * 8:k * 8 + 8], conv_ps[:, h % 2], ACT.Identity,
                                     bias=V["b_s3"], accum_out=ssum2[:, g, k:k + 1]).then_inc(evac, 1)

            def square2(u, s, j):
                g = 2 * (s % 2) + j
                n = 2 * u + j
                act.wait_ge(mean2_mm, n + 1)
                if later(n, 4):
                    act.wait_ge(aff2, 4 * (n - 4) + 4)
                nc.scalar.activation(share2[:, g], gn2_ps[:, 0:2], ACT.Copy, scale=-1.0,
                                     accum_out=negm2[:, g:g + 1]).then_inc(negm2_done, 1)
                act.wait_ge(negm2_done, n + 1)
                act.wait_ge(evac, 2 * n + 2)
                if later(n, 1):
                    act.wait_ge(sq2_done, n)
                nc.scalar.activation(junk[:, 2], sp_buf[:, g].rearrange("p b w -> p (b w)"), ACT.Square,
                                     bias=negm2[:, g:g + 1], accum_out=ssq2[:, g:g + 1]).then_inc(sq2_done, 1)

            def variance2(u, s, j):
                g = 2 * (s % 2) + j
                n = 2 * u + j
                act.wait_ge(var2_mm, n + 1)
                if later(n, 4):
                    act.wait_ge(aff2, 4 * (n - 4) + 1)
                nc.scalar.activation(var2_e[:, g:g + 1], gn2_ps[:, 2:3], ACT.Identity,
                                     bias=consts[:, 6:7]).then_inc(var2_done, 1)

            def spatial_gate(u, s, j):
                g = 2 * (s % 2) + j
                n = 2 * u + j
                act.wait_ge(aff2, 4 * n + 4)
                act.wait_ge(sq2_done, n + 1)
                flat = sp_buf[:, g].rearrange("p b w -> p (b w)")
                nc.scalar.activation(flat, flat, ACT.Sigmoid, scale=scale2[:, g:g + 1],
                                     bias=bias2[:, g:g + 1]).then_inc(sig2, 1)

            def body(t, q):
                a, sa = t + 1, (q + 1) % XS
                da = sa % 2
                b, sb_ = t - 1, (q - 1) % XS
                if real(b):
                    evacuate(b, sb_, 3)
                if real(a):
                    act.wait_ge(mean_mm, a + 1)
                    if later(a, 4):
                        act.wait_ge(final, 2 * (a - XS) + 2)
                    nc.scalar.activation(negm[:, sa], norm_ps[:, 0:2], ACT.Copy, scale=-1.0).then_inc(negm_done, 1)
                    act.wait_ge(negm_done, a + 1)
                    for j in range(2):
                        act.wait_ge(x_in[sa][j], 4 * RB * (a - sa) + 16 * RB)
                        if later(a, 1):
                            act.wait_ge(sq_done, 2 * a + j - 1)
                        nc.scalar.activation(junk[:, j], xt[:, sa, j].rearrange("p b w -> p (b w)"), ACT.Square,
                                             bias=negm[:, sa, j:j + 1],
                                             accum_out=ssq[:, da, j:j + 1]).then_inc(sq_done, 1)
                if real(b):
                    square2(b, sb_, 1)
                if real(t):
                    evacuate(t, q, 0)
                if real(a):
                    pos = pos_ps[:, 0:2 * (NB + W)].rearrange("p (j n) -> p j n", j=2)
                    act.wait_ge(pos_mm, a + 1)
                    act.wait_ge(rstd_done, a + 1)
                    for j in range(2):
                        nc.scalar.activation(gate_h[:, da, j], pos[:, j, 0:NB], ACT.Sigmoid,
                                             scale=rstd[:, sa, j:j + 1], bias=b_pos[:, 0:1]).then_inc(gates_done, 1)
                    if later(a, 2):
                        act.wait_ge(gp_dve, 2 * (a - 1))
                    for j in range(2):
                        nc.scalar.activation(gate_w[:, da, j], pos[:, j, NB:NB + W], ACT.Sigmoid,
                                             scale=rstd[:, sa, j:j + 1], bias=b_pos[:, 1:2]).then_inc(gates_done, 1)

                def gate_products(j):
                    if real(a):
                        act.wait_ge(ghr_done, a + 1)
                        act.wait_ge(gates_done, 4 * a + 4)
                        if later(a, 2):
                            act.wait_ge(conv_mm, 4 * (a - 2) + 4)
                        for i in range(ACT_BANDS):
                            ins = nc.scalar.activation(gated[:, da, j, i, 1:1 + W], gate_w[:, da, j], ACT.Copy,
                                                       scale=gate_hr[:, da, j, i:i + 1])
                        ins.then_inc(gp_act, 1)

                if real(b):
                    variance2(b, sb_, 1)
                gate_products(0)
                if real(t):
                    evacuate(t, q, 1)
                gate_products(1)
                if real(b):
                    spatial_gate(b, sb_, 1)
                if real(t):
                    square2(t, q, 0)
                if real(a):
                    act.wait_ge(cgn, 9 * a + 9)
                    if later(a, 2):
                        act.wait_ge(kfac_done, a - 1)
                    nc.scalar.activation(cgate[:, da], ch[:, 9], ACT.Sigmoid).then_inc(cgate_done, 1)
                if real(t):
                    evacuate(t, q, 2)
                    variance2(t, q, 0)
                    spatial_gate(t, q, 0)

            turns(act, body)

        @block.vector
        def _(dve):
            made = [0]

            def link(ins):
                made[0] += 1
                ins.then_inc(w_dve, 1)
                dve.wait_ge(w_dve, made[0])

            dve.wait_ge(w_in, 16 * 19)
            def expand(dst, rep, mask, parts=P):
                link(nc.vector.tensor_tensor(dst.rearrange("p (o r) -> p o r", r=RB),
                                             rep.unsqueeze(2).to_broadcast([parts, CG, RB]),
                                             mask.unsqueeze(1).to_broadcast([parts, CG, RB]), ALU.mult))

            for kw in range(KW):
                expand(W_conv[:, kw], wconv_rep[:, kw, 1], masks[:, 1])
                for i, kh in enumerate((0, 2)):
                    expand(w_part[:, i, kw], wconv_rep[:, kw, kh], masks[:, kh])
                    link(nc.vector.tensor_tensor(W_conv[:, kw], W_conv[:, kw], w_part[:, i, kw], ALU.add))
            expand(W_halo[:, :], whalo_in[:, :], hmask[:, :], HALO)
            expand(W_s1h[:, :], ws1_rep[:, :], masks[:, 1])
            expand(W_ph[:, :], wph_rep[:, :], masks[:, 1])
            expand(W_pw[:, :], wpw_rep[:, :], masks[:, 1])
            expand(W_gmp[:, :], wcc_rep[:, 1], masks[:, 1])
            for dst, rep in ((W_s1w, ws1_rep[:, :]), (W_gap, wcc_rep[:, 0])):
                link(nc.vector.tensor_scalar(dst[:, :].rearrange("p (o r) -> p o r", r=RB),
                                             rep.unsqueeze(2).to_broadcast([P, CG, RB]), 1.0 / RB, None, ALU.mult))
            link(nc.vector.tensor_scalar(M_chan[:, :], S_chan[:, :], 1.0 / PIX, None, ALU.mult))
            dve.wait_ge(w_pe, 1)
            link(nc.vector.tensor_copy(W_rows[:, :], pos_ps[:, 0:P]))
            link(nc.vector.tensor_copy(W_cols[:, :], pos_ps[:, P:2 * P]))
            link(nc.vector.tensor_tensor(b_pos[:, :], pos_ps[:, 2 * P:2 * P + 2], vec[:, 4:6], ALU.add))
            for s in range(2):
                for col in (0, WP - 1):
                    link(nc.vector.memset(gated[:, s, :, :, col:col + 1], 0.0))

            def finish(u, s, j):
                g = 2 * (s % 2) + j
                n = 2 * u + j
                flat = sp_buf[:, g].rearrange("p b w -> p (b w)")
                xf = xt[:, s, j].rearrange("p b w -> p (b w)")
                dve.wait_ge(sig2, n + 1)
                nc.vector.scalar_tensor_tensor(flat, xf, negm[:, s, j:j + 1], flat, ALU.add, ALU.mult).then_inc(fin_a, 1)
                dve.wait_ge(fin_a, n + 1)
                dve.wait_ge(kfac_done, u + 1)
                nc.vector.scalar_tensor_tensor(flat, flat, kfac[:, s, j:j + 1], xf, ALU.mult, ALU.add).then_inc(final, 1)

            def body(t, q):
                a, sa = t + 1, (q + 1) % XS
                da = sa % 2
                b, sb_ = t - 1, (q - 1) % XS
                c, sc = t + 2, (q + 2) % XS
                dc = sc % 2
                if real(b):
                    finish(b, sb_, 0)
                if real(a):
                    dve.wait_ge(negm_done, a + 1)
                    if later(a, 2):
                        dve.wait_ge(pos_mm, a - 1)
                    for j in range(2):
                        nc.vector.tensor_scalar(sums_n[:, da, j, 0:NB], sums[:, da, j, 0:NB], 1.0 / W,
                                                negm[:, sa, j:j + 1], ALU.mult, ALU.add)
                        ins = nc.vector.tensor_scalar(sums_n[:, da, j, NB:], sums[:, da, j, NB:], 1.0 / NB,
                                                      negm[:, sa, j:j + 1], ALU.mult, ALU.add)
                    ins.then_inc(sn_done, 1)
                def row_sums(j):
                    if real(c):
                        if later(c, 2):
                            dve.wait_ge(sn_done, c - 1)
                        dve.wait_ge(x_in[sc][j], 4 * RB * (c - sc) + 16 * RB)
                        nc.vector.tensor_reduce(sums[:, dc, j, 0:NB], xt[:, sc, j], AX_X,
                                                ALU.add).then_inc(sums_done, 1)

                def column_sums(j):
                    if real(c):
                        nc.vector.tensor_reduce(sums[:, dc, j, NB:], xt[:, sc, j].rearrange("p b w -> p w b"), AX_X,
                                                ALU.add).then_inc(sums_done, 1)

                def modulate(j):
                    if real(a):
                        dve.wait_ge(gp_act, 2 * a + j + 1)
                        dve.wait_ge(gp_dve, 2 * a + j + 1)
                        nc.vector.scalar_tensor_tensor(gated[:, da, j, :, 1:1 + W], xt[:, sa, j],
                                                       negm[:, sa, j:j + 1], gated[:, da, j, :, 1:1 + W],
                                                       ALU.add, ALU.mult).then_inc(mod_done, 1)

                row_sums(0)
                if real(a):
                    dve.wait_ge(mxs_mm, a + 1)
                    if later(a, 2):
                        dve.wait_ge(cin, 3 * (a - 1))
                    nc.vector.tensor_reduce(gmx[:, da], cw_ps[:, 0:2 * RB].rearrange("p (j r) -> p j r", j=2),
                                            AX_X, ALU.max).then_inc(gmx_done, 1)
                    dve.wait_ge(var_mm, a + 1)
                    if later(a, 2):
                        dve.wait_ge(rstd_done, a - 1)
                    nc.vector.tensor_scalar(var_e[:, da], norm_ps[:, 2:4], EPS, None, ALU.add).then_inc(var_done, 1)
                row_sums(1)
                if real(c):
                    dve.wait_ge(sums_done, 4 * c + 2)
                    if later(c, 2):
                        dve.wait_ge(cin, 3 * (c - 2) + 1)
                    nc.vector.tensor_reduce(tot[:, dc], sums[:, dc, :, 0:NB], AX_X, ALU.add).then_inc(tot_done, 1)
                if real(a):
                    dve.wait_ge(gates_done, 4 * a + 4)
                    dve.wait_ge(rstd_done, a + 1)
                    if later(a, 2):
                        dve.wait_ge(gp_act, 2 * (a - 1))
                    nc.vector.tensor_tensor(gate_hr[:, da], gate_h[:, da],
                                            rstd[:, sa].unsqueeze(2).to_broadcast([P, 2, NB]),
                                            ALU.mult).then_inc(ghr_done, 1)
                    dve.wait_ge(ghr_done, a + 1)
                    if later(a, 2):
                        dve.wait_ge(conv_mm, 4 * (a - 2) + 4)
                    for j in range(2):
                        nb = NB - ACT_BANDS
                        nc.vector.tensor_tensor(gated[:, da, j, ACT_BANDS:, 1:1 + W],
                                                gate_w[:, da, j].unsqueeze(1).to_broadcast([P, nb, W]),
                                                gate_hr[:, da, j, ACT_BANDS:].unsqueeze(2).to_broadcast([P, nb, W]),
                                                ALU.mult).then_inc(gp_dve, 1)
                column_sums(0)
                column_sums(1)
                if real(a):
                    dve.wait_ge(ch_mm, a + 1)
                    if later(a, 1):
                        dve.wait_ge(cgn, 9 * (a - 1) + 1)
                    nc.vector.tensor_tensor(ch[:, 0], cw_ps[:, 16:18], rstd[:, sa], ALU.mult).then_inc(ch_done, 1)
                if real(c):
                    if later(c, 1):
                        dve.wait_ge(mxx_done, c)
                    nc.vector.tensor_reduce(mx[:, dc], xt[:, sc].rearrange("p j b w -> p j (b w)"), AX_X,
                                            ALU.max).then_inc(mx_done, 1)
                    dve.wait_ge(mx_done, c + 1)
                    if later(c, 2):
                        dve.wait_ge(mxs_mm, c - 1)
                    nc.vector.tensor_tensor(mx_x[:, dc], mx[:, dc].unsqueeze(2).to_broadcast([P, 2, RB]),
                                            masks[:, 1].unsqueeze(1).to_broadcast([P, 2, RB]),
                                            ALU.mult).then_inc(mxx_done, 1)
                modulate(0)
                modulate(1)
                if real(b):
                    finish(b, sb_, 1)

            turns(dve, body)

        @block.tensor
        def _(pe):
            pe.wait_ge(w_dve, 23)
            nc.tensor.matmul(pos_ps[:, 0:P], W_s1h[:, :], W_ph[:, :], start=True, stop=True)
            nc.tensor.matmul(pos_ps[:, P:2 * P], W_s1w[:, :], W_pw[:, :], start=True, stop=True)
            nc.tensor.matmul(pos_ps[:, 2 * P:2 * P + 1], W_ph[:, :], V["b_s1"], start=True, stop=True)
            nc.tensor.matmul(pos_ps[:, 2 * P + 1:2 * P + 2], W_pw[:, :], V["b_s1"], start=True,
                             stop=True).then_inc(w_pe, 1)
            pe.wait_ge(w_dve, 26)
            pe.wait_ge(w_pool, 6)

            pos = pos_ps[:, 0:2 * (NB + W)].rearrange("p (j n) -> p j n", j=2)

            def mm(ps, lhsT, rhs, start=True, stop=True):
                return nc.tensor.matmul(ps, lhsT, rhs, start=start, stop=stop)

            def body(t, q):
                a, sa = t + 1, (q + 1) % XS
                da = sa % 2
                b, sb_ = t - 1, (q - 1) % XS

                def mean():
                    if real(a):
                        pe.wait_ge(tot_done, a + 1)
                        if later(a, 1):
                            pe.wait_ge(var_done, a)
                        mm(norm_ps[:, 0:2], M_all[:, :], tot[:, da]).then_inc(mean_mm, 1)

                def maxima():
                    if real(a):
                        pe.wait_ge(mxx_done, a + 1)
                        if later(a, 1):
                            pe.wait_ge(ch_done, a)
                        mm(cw_ps[:, 0:2 * RB], S_chan[:, :], mx_x[:, da].rearrange("p j r -> p (j r)")).then_inc(mxs_mm, 1)

                def mean2(u, s, j):
                    if real(u):
                        g = 2 * (s % 2) + j
                        n = 2 * u + j
                        pe.wait_ge(evac, 2 * n + 2)
                        if later(n, 1):
                            pe.wait_ge(var2_done, n)
                        mm(gn2_ps[:, 0:2], M_chan[:, :], ssum2[:, g]).then_inc(mean2_mm, 1)

                def var2(u, s, j):
                    if real(u):
                        g = 2 * (s % 2) + j
                        n = 2 * u + j
                        pe.wait_ge(sq2_done, n + 1)
                        pe.wait_ge(negm2_done, n + 1)
                        mm(gn2_ps[:, 2:3], M_chan[:, :], ssq2[:, g:g + 1]).then_inc(var2_mm, 1)

                def var_pos1():
                    if real(a):
                        pe.wait_ge(sq_done, 2 * a + 2)
                        pe.wait_ge(negm_done, a + 1)
                        mm(norm_ps[:, 2:4], M_all[:, :], ssq[:, da]).then_inc(var_mm, 1)
                        pe.wait_ge(sn_done, a + 1)
                        if later(a, 1):
                            pe.wait_ge(gates_done, 4 * a)
                        mm(pos[:, :, 0:NB], W_rows[:, :], sums_n[:, da, :, 0:NB])
                        mm(pos[:, :, NB:NB + W], W_cols[:, :], sums_n[:, da, :, NB:]).then_inc(pos_mm, 1)

                def channel():
                    if real(a):
                        pe.wait_ge(cin, 3 * a + 3)
                        pe.wait_ge(gmx_done, a + 1)
                        mm(cw_ps[:, 16:18], W_gap[:, :], gap_n[:, da], stop=False)
                        mm(cw_ps[:, 16:18], W_gmp[:, :], gmx_n[:, da], start=False).then_inc(ch_mm, 1)

                def conv(h, first, last):
                    if not real(t):
                        return
                    j, k = h // 2, h % 2
                    d = q % 2
                    if first == 0:
                        pe.wait_ge(mod_done, 2 * t + j + 1)
                        if later(4 * t + h, 2):
                            pe.wait_ge(evac, 4 * t + h - 1)
                    for i in range(first, last):
                        w, bank = i // 2, i % 2
                        band = (2 * k + bank) * BB
                        o = conv_ps[:, h % 2, bank * BB:(bank + 1) * BB]
                        if w < KW:
                            mm(o, W_conv[:, w], gated[:, d, j, band:band + BB, w:w + W],
                               start=w == 0, stop=False)
                        else:
                            if bank == 0:
                                pe.wait_ge(halo_in[d][j], 16 * (t - d) + 32)
                            rows = halo[:, d, j].rearrange("p (b w) -> p b w", w=WP)
                            ins = mm(o, W_halo[:, :], rows[:, band:band + BB, 0:W], start=False)
                    if last == 8:
                        ins.then_inc(conv_mm, 1)

                mean()
                conv(0, 0, 2)
                mean2(b, sb_, 1)
                conv(0, 2, 4)
                maxima()
                conv(0, 4, 7)
                var_pos1()
                conv(0, 7, 8)
                conv(1, 0, 1)
                var2(b, sb_, 1)
                conv(1, 1, 7)
                channel()
                conv(1, 7, 8)
                conv(2, 0, 3)
                mean2(t, q, 0)
                conv(2, 3, 8)
                conv(3, 0, 3)
                var2(t, q, 0)
                conv(3, 3, 8)

            turns(pe, body)


_VECS = ["b_cc", "gn1_w", "gn1_b", "b_s1", "b_ph", "b_pw", "b_s3", "gn2_w", "gn2_b"]


def kernel(**inputs):
    import numpy as np
    import concourse.bacc as bacc
    from concourse.bass_utils import run_bass_kernel_spmd

    def get(name):
        return np.asarray(inputs["L0_conv_" + name])

    r = np.arange(P) % RB
    o = np.arange(RB)
    same_channel = (np.arange(P)[:, None] // RB == np.arange(P)[None, :] // RB).astype(np.float32)
    row_masks = np.stack([o[None, :] == (r[:, None] + 1 - kh) for kh in range(3)], 1).astype(np.float32)
    halo_mask = np.zeros((HALO, RB), np.float32)
    halo_mask[:HALO // 2, 0] = 1
    halo_mask[HALO // 2:, RB - 1] = 1
    arrays = {
        "x": np.asarray(inputs["x"]),
        "wcc": get("w_cc").reshape(CG, 2, CG).transpose(2, 1, 0).reshape(CG, 2 * CG),
        "wconv": get("w_s3").transpose(1, 3, 2, 0).reshape(CG, KW * 3 * CG),
        "ws1": get("w_s1"),
        "wph": get("w_ph").T,
        "wpw": get("w_pw").T,
        **{n: get(n) for n in _VECS},
        "same_channel": same_channel,
        "row_masks": row_masks.reshape(P, 3 * RB),
        "halo_mask": halo_mask,
    }
    arrays = {f"in_{n}": np.ascontiguousarray(a) for n, a in arrays.items()}
    nc = bacc.Bacc("TRN2", target_bir_lowering=False, num_devices=1)
    t = {n[3:]: nc.dram_tensor(n, a.shape, mybir.dt.from_np(a.dtype), kind="ExternalInput").ap()
         for n, a in arrays.items()}
    out = nc.dram_tensor("out_0", (N, C, HT, W), F32, kind="ExternalOutput").ap()
    conv_attention(nc, t["x"], t["wcc"], t["wconv"], t["ws1"], t["wph"], t["wpw"], [t[n] for n in _VECS],
                   t["same_channel"], t["row_masks"], t["halo_mask"], out)
    res = run_bass_kernel_spmd(nc, [arrays], core_ids=[0])
    return res.results[0]["out_0"]
```

```python
from contextlib import ExitStack

import concourse.bass as bass
from concourse import mybir

F32 = mybir.dt.float32
BF16 = mybir.dt.bfloat16
ALU = mybir.AluOpType
ACT = mybir.ActivationFunctionType
AX_X = mybir.AxisListType.X

P = 128
N, C, HT, W = 8, 512, 128, 128
CG = 16
RB = P // CG
NB = HT // RB
GROUPS = N * C // CG
PIX = HT * W
WP = W + 2
UNITS = GROUPS // 2
XS = 4
EPS = 1e-5
KW = 3
HALO = 2 * CG * KW
HALF = 2
BB = 4
RUN = (NB - 2) * WP + W
ACT_BANDS = 14
W_LOADS = 6
PER = 4


def conv_attention(nc, x, by_channel, wconv, same_channel, row_masks, halo_mask, out):
    x_g = x.rearrange("n (g c) (b r) w -> (n g) r c b w", c=CG, r=RB)
    out_g = out.rearrange("n (g c) (b r) w -> (n g) r c b w", c=CG, r=RB)

    with ExitStack() as ctx:
        def sb(name, shape, dt=F32):
            return ctx.enter_context(nc.sbuf_tensor(name, shape, dt))

        def psum(name, shape):
            return ctx.enter_context(nc.psum_tensor(name, shape, F32))

        def sem(name):
            return ctx.enter_context(nc.semaphore(name))

        xt = sb("xt", [P, XS, 2, NB, W])
        gated = sb("gated", [P, 2, 2, NB, WP])
        halo = sb("halo", [HALO, 2, 2, NB * WP])
        sp_buf = sb("sp_buf", [P, 4, NB, W])
        junk = sb("junk", [P, 3, NB * W], BF16)
        weights = sb("weights", [P, by_channel.shape[1]])
        whalo_in = sb("whalo_in", [HALO, CG])
        masks = sb("masks", [P, 3, RB])
        hmask = sb("hmask", [HALO, RB])
        mask_pix = sb("mask_pix", [P, RB])
        W_conv = sb("W_conv", [P, KW, P])
        w_part = sb("w_part", [P, 2, KW, P])
        W_halo = sb("W_halo", [HALO, P])
        W_s1h = sb("W_s1h", [P, P])
        W_s1w = sb("W_s1w", [P, P])
        W_rows = sb("W_rows", [P, P])
        W_cols = sb("W_cols", [P, P])
        b_pos = sb("b_pos", [P, 2])
        W_ph = sb("W_ph", [P, P])
        W_pw = sb("W_pw", [P, P])
        W_gap = sb("W_gap", [P, P])
        W_gmp = sb("W_gmp", [P, P])
        M_all = sb("M_all", [P, P])
        M_chan = sb("M_chan", [P, P])
        S_chan = sb("S_chan", [P, P])
        sums = sb("sums", [P, 2, 2, NB + W])
        sums_n = sb("sums_n", [P, 2, 2, NB + W])
        tot = sb("tot", [P, 2, 2])
        mx = sb("mx", [P, 2, 2])
        spread_in = sb("spread_in", [P, 2, 2 + 2 * RB])
        gmx = sb("gmx", [P, 2, 2])
        gap_n = sb("gap_n", [P, 2, 2])
        gmx_n = sb("gmx_n", [P, 2, 2])
        gap_s = sb("gap_s", [P, 2, 2])
        negm = sb("negm", [P, 4, 2])
        ssq = sb("ssq", [P, 2, 2])
        var_e = sb("var_e", [P, 2, 2])
        rstd = sb("rstd", [P, 4, 2])
        gate_h = sb("gate_h", [P, 2, 2, NB])
        gate_hr = sb("gate_hr", [P, 2, 2, NB])
        gate_w = sb("gate_w", [P, 2, 2, W])
        ch = sb("ch", [P, 10, 2])
        cgate = sb("cgate", [P, 2, 2])
        kfac = sb("kfac", [P, 4, 2])
        consts = sb("consts", [P, 8])
        ssum2_first = sb("ssum2_first", [P, 2, 2])
        share2 = sb("share2", [P, 4, 2])
        negm2 = sb("negm2", [P, 4])
        ssq2 = sb("ssq2", [P, 4])
        var2_e = sb("var2_e", [P, 4])
        rstd2 = sb("rstd2", [P, 4])
        scale2 = sb("scale2", [P, 4])
        sh2 = sb("sh2", [P, 4])
        bias2 = sb("bias2", [P, 4])

        conv_ps = psum("conv_ps", [P, 2, HALF * BB, W])
        norm_ps = psum("norm_ps", [P, 512])
        pos_ps = psum("pos_ps", [P, 512])
        gn2_ps = psum("gn2_ps", [P, 512])
        cw_ps = psum("cw_ps", [P, 512])

        w_in = sem("w_in")
        w_dve = sem("w_dve")
        w_pe = sem("w_pe")
        w_pool = sem("w_pool")
        x_in = [[sem(f"x_in{s}{j}") for j in range(2)] for s in range(XS)]
        halo_in = [[sem(f"halo_in{s}{j}") for j in range(2)] for s in range(2)]
        stored = [sem(f"stored{s}") for s in range(4)]
        sums_done = sem("sums_done")
        tot_done = sem("tot_done")
        mx_done = sem("mx_done")
        mxx_done = sem("mxx_done")
        mean_mm = sem("mean_mm")
        negm_done = sem("negm_done")
        sq_done = sem("sq_done")
        var_mm = sem("var_mm")
        var_done = sem("var_done")
        rstd_done = sem("rstd_done")
        sn_done = sem("sn_done")
        pos_mm = sem("pos_mm")
        gates_done = sem("gates_done")
        ghr_done = sem("ghr_done")
        gp_act = sem("gp_act")
        gp_dve = sem("gp_dve")
        mod_done = sem("mod_done")
        conv_mm = sem("conv_mm")
        evac = sem("evac")
        mean2_mm = sem("mean2_mm")
        spread_mm = sem("spread_mm")
        negm2_done = sem("negm2_done")
        sq2_done = sem("sq2_done")
        var2_mm = sem("var2_mm")
        var2_done = sem("var2_done")
        aff2 = sem("aff2")
        sig2 = sem("sig2")
        fin_a = sem("fin_a")
        final = sem("final")
        gmx_done = sem("gmx_done")
        cin = sem("cin")
        ch_mm = sem("ch_mm")
        ch_done = sem("ch_done")
        cgn = sem("cgn")
        cgate_done = sem("cgate_done")
        kfac_done = sem("kfac_done")

        def later(n, first):
            return not isinstance(n, int) or n >= first

        def real(u):
            return not isinstance(u, int) or 0 <= u < UNITS

        def ssum2(s, j):
            return ssum2_first[:, s % 2] if j == 0 else spread_in[:, s % 2, 0:2]

        def turns(eng, body):
            first, last = 1, (UNITS - 4) // PER
            for t in range(-3, first * PER):
                body(t, t % PER)
            with eng.Fori(first, last) as turn:
                for q in range(PER):
                    body(turn * PER + q, q)
            for t in range(last * PER, UNITS + 1):
                body(t, t % PER)

        ends = [0]
        for k in (2 * CG, KW * 3 * CG, CG, CG, CG, len(_VECS)):
            ends.append(ends[-1] + k)
        wcc_rep, wconv_rep, ws1_rep, wph_rep, wpw_rep, vec = [
            weights[:, i:e] for i, e in zip(ends[:-1], ends[1:])]
        wcc_rep = wcc_rep.rearrange("p (s o) -> p s o", s=2)
        wconv_rep = wconv_rep.rearrange("p (kw kh o) -> p kw kh o", kw=KW, kh=3)
        V = {n: vec[:, i:i + 1] for i, n in enumerate(_VECS)}

        MAXIMA = slice(2, 2 + 2 * RB)
        VAR2 = slice(2 + 2 * RB, 3 + 2 * RB)

        block = ctx.enter_context(nc.Block())

        @block.sync
        def _(sp):
            sp.dma_start(weights[:].rearrange("p k -> p () k"), by_channel.rearrange("c k -> c () k").to_broadcast(
                [CG, RB, by_channel.shape[1]])).then_inc(w_in, 16)
            hv = wconv.rearrange("c (kw kh o) -> (c kw) kh o", kw=KW, kh=3)
            sp.dma_start(whalo_in[0:HALO // 2, :], hv[:, 0, :]).then_inc(w_in, 16)
            sp.dma_start(whalo_in[HALO // 2:HALO, :], hv[:, 2, :]).then_inc(w_in, 16)
            sp.dma_start(S_chan[:, :], same_channel).then_inc(w_in, 16)
            sp.dma_start(masks[:], row_masks).then_inc(w_in, 16)
            sp.dma_start(hmask[:, :], halo_mask).then_inc(w_in, 16)

            def body(t, q):
                u, s = t - 1, (q - 1) % XS
                v, vs = t + 3, (q + 3) % XS
                h, hs = t + 1, (q + 1) % 2

                def group(rows, n):
                    size = CG * PIX
                    at = n * size if isinstance(n, int) else sp.snap(n * size)
                    first = rows[0, 0]
                    return [bass.AP(tensor=first.tensor, offset=at + r * W, ap=[list(d) for d in first.ap])
                            for r in range(RB)]

                def load(j):
                    if real(v):
                        come = group(x_g, 2 * v + j)
                        if later(v, XS):
                            sp.wait_ge(final, 2 * (v - XS) + j + 1)
                        for r in range(RB):
                            sp.dma_start(xt[r:P:RB, vs, j], come[r]).then_inc(x_in[vs][j], 16)

                def store(j):
                    if real(u):
                        g = 2 * (s % 2) + j
                        to = group(out_g, 2 * u + j)
                        sp.wait_ge(final, 2 * u + j + 1)
                        for r in range(RB):
                            sp.dma_start(to[r], sp_buf[r:P:RB, g]).then_inc(stored[g], 16)

                def halo_rows(j):
                    if real(h):
                        flat = gated[:, hs, j].rearrange("p b w -> p (b w)")
                        sp.wait_ge(mod_done, 2 * h + j + 1)
                        for side in range(2):
                            row = RB - 1 if side == 0 else 0
                            src = flat[row:P:RB, 0:NB * WP]
                            at = 0 if side == 0 else WP
                            shifts = bass.AP(tensor=src.tensor, offset=src.offset + at,
                                             ap=[list(src.ap[0]), [1, KW], [1, RUN]])
                            to = WP if side == 0 else 0
                            sp.dma_start(halo[side * CG * KW:(side + 1) * CG * KW, hs, j, to:to + RUN],
                                         shifts).then_inc(halo_in[hs][j], 16)

                load(0)
                store(0)
                halo_rows(0)
                halo_rows(1)
                load(1)
                store(1)

            turns(sp, body)
            for g in range(4):
                sp.wait_ge(stored[g], 16 * RB * (GROUPS // 4))

        @block.gpsimd
        def _(pool):
            nc.gpsimd.memset(M_all[:, :], 1.0 / (CG * PIX)).then_inc(w_pool, 1)
            for i, value in enumerate((-0.5, 1.0 / (NB * W), 1.0, EPS)):
                nc.gpsimd.memset(consts[:, 2 * i:2 * i + 2], value).then_inc(w_pool, 1)
            nc.gpsimd.memset(halo[:], 0.0).then_inc(w_pool, 1)
            pool.wait_ge(w_pool, 6)
            pool.wait_ge(w_in, 16 * W_LOADS)

            def affine2(u, s, j):
                g = 2 * (s % 2) + j
                n = 2 * u + j
                pool.wait_ge(var2_done, n + 1)
                if later(n, 4):
                    pool.wait_ge(sig2, n - 3)
                nc.gpsimd.tensor_tensor(rstd2[:, g:g + 1], var2_e[:, g:g + 1], consts[:, 0:1],
                                        ALU.pow).then_inc(aff2, 1)
                pool.wait_ge(aff2, 4 * n + 1)
                nc.gpsimd.tensor_tensor(scale2[:, g:g + 1], rstd2[:, g:g + 1], V["gn2_w"],
                                        ALU.mult).then_inc(aff2, 1)
                pool.wait_ge(aff2, 4 * n + 2)
                nc.gpsimd.tensor_tensor(sh2[:, g:g + 1], scale2[:, g:g + 1], negm2[:, g:g + 1],
                                        ALU.mult).then_inc(aff2, 1)
                pool.wait_ge(aff2, 4 * n + 3)
                nc.gpsimd.tensor_tensor(bias2[:, g:g + 1], sh2[:, g:g + 1], V["gn2_b"],
                                        ALU.add).then_inc(aff2, 1)

            def channel_in(u, s):
                d = s % 2
                pool.wait_ge(tot_done, u + 1)
                if later(u, 2):
                    pool.wait_ge(ch_mm, u - 1)
                nc.gpsimd.tensor_tensor(gap_s[:, d], tot[:, d], consts[:, 2:4], ALU.mult).then_inc(cin, 1)
                pool.wait_ge(cin, 3 * u + 1)
                pool.wait_ge(negm_done, u + 1)
                nc.gpsimd.tensor_tensor(gap_n[:, d], gap_s[:, d], negm[:, s], ALU.add).then_inc(cin, 1)
                pool.wait_ge(gmx_done, u + 1)
                nc.gpsimd.tensor_tensor(gmx_n[:, d], gmx[:, d], negm[:, s], ALU.add).then_inc(cin, 1)

            def channel_norm(u, s):
                pool.wait_ge(ch_done, u + 1)

                if later(u, 1):
                    pool.wait_ge(cgate_done, u)
                nc.gpsimd.tensor_tensor(ch[:, 1], ch[:, 0], V["b_cc"].to_broadcast([P, 2]), ALU.add).then_inc(cgn, 1)
                pool.wait_ge(cgn, 9 * u + 1)
                nc.gpsimd.tensor_tensor(ch[:, 2], ch[:, 1], consts[:, 4:6], ALU.mult).then_inc(cgn, 1)
                pool.wait_ge(cgn, 9 * u + 2)
                nc.gpsimd.tensor_tensor(ch[:, 3], ch[:, 1], ch[:, 2], ALU.subtract).then_inc(cgn, 1)
                pool.wait_ge(cgn, 9 * u + 3)
                nc.gpsimd.tensor_tensor(ch[:, 4], ch[:, 3], ch[:, 3], ALU.mult).then_inc(cgn, 1)
                pool.wait_ge(cgn, 9 * u + 4)
                nc.gpsimd.tensor_tensor(ch[:, 5], ch[:, 4], consts[:, 6:8], ALU.add).then_inc(cgn, 1)
                pool.wait_ge(cgn, 9 * u + 5)
                nc.gpsimd.tensor_tensor(ch[:, 6], ch[:, 5], consts[:, 0:2], ALU.pow).then_inc(cgn, 1)
                pool.wait_ge(cgn, 9 * u + 6)
                nc.gpsimd.tensor_tensor(ch[:, 7], ch[:, 3], ch[:, 6], ALU.mult).then_inc(cgn, 1)
                pool.wait_ge(cgn, 9 * u + 7)
                nc.gpsimd.tensor_tensor(ch[:, 8], ch[:, 7], V["gn1_w"].to_broadcast([P, 2]), ALU.mult).then_inc(cgn, 1)
                pool.wait_ge(cgn, 9 * u + 8)
                nc.gpsimd.tensor_tensor(ch[:, 9], ch[:, 8], V["gn1_b"].to_broadcast([P, 2]), ALU.add).then_inc(cgn, 1)

            def body(t, q):
                a, sa = t + 1, (q + 1) % XS
                b, sb_ = t - 1, (q - 1) % XS
                if real(a):
                    pool.wait_ge(var_done, a + 1)
                    if later(a, 4):
                        pool.wait_ge(final, 2 * (a - XS) + 2)
                    nc.gpsimd.tensor_tensor(rstd[:, sa], var_e[:, sa % 2], consts[:, 0:2],
                                            ALU.pow).then_inc(rstd_done, 1)
                if real(b):
                    affine2(b, sb_, 1)
                if real(a):
                    channel_in(a, sa)
                    channel_norm(a, sa)
                if real(t):
                    affine2(t, q, 0)
                if real(a):
                    pool.wait_ge(cgate_done, a + 1)
                    pool.wait_ge(rstd_done, a + 1)
                    nc.gpsimd.tensor_tensor(kfac[:, sa], cgate[:, sa % 2], rstd[:, sa],
                                            ALU.mult).then_inc(kfac_done, 1)

            turns(pool, body)

        @block.scalar
        def _(act):
            act.wait_ge(w_in, 16 * W_LOADS)
            act.wait_ge(w_pool, 6)

            def evacuate(u, s, h):
                j, k = h // 2, h % 2
                g = 2 * (s % 2) + j
                act.wait_ge(conv_mm, 4 * u + h + 1)
                if k == 0:
                    if later(u, 2):
                        act.wait_ge(stored[g], 8 * RB * (u - s % 2))
                nc.scalar.activation(sp_buf[:, g, k * 8:k * 8 + 8], conv_ps[:, h % 2], ACT.Identity,
                                     bias=V["b_s3"], accum_out=ssum2(s, j)[:, k:k + 1]).then_inc(evac, 1)

            def square2(u, s, j):
                g = 2 * (s % 2) + j
                n = 2 * u + j
                if j == 0:
                    act.wait_ge(mean2_mm, u + 1)
                else:
                    act.wait_ge(spread_mm, u + 3)
                if later(n, 4):
                    act.wait_ge(aff2, 4 * (n - 4) + 4)
                nc.scalar.activation(share2[:, g], gn2_ps[:, 0:2], ACT.Copy, scale=-1.0,
                                     accum_out=negm2[:, g:g + 1]).then_inc(negm2_done, 1)
                act.wait_ge(negm2_done, n + 1)
                act.wait_ge(evac, 2 * n + 2)
                if later(n, 1):
                    act.wait_ge(sq2_done, n)
                nc.scalar.activation(junk[:, 2], sp_buf[:, g].rearrange("p b w -> p (b w)"), ACT.Square,
                                     bias=negm2[:, g:g + 1], accum_out=ssq2[:, g:g + 1]).then_inc(sq2_done, 1)

            def variance2(u, s, j):
                g = 2 * (s % 2) + j
                n = 2 * u + j
                act.wait_ge(var2_mm, n + 1)
                if later(n, 4):
                    act.wait_ge(aff2, 4 * (n - 4) + 1)
                nc.scalar.activation(var2_e[:, g:g + 1], gn2_ps[:, VAR2], ACT.Identity,
                                     bias=consts[:, 6:7]).then_inc(var2_done, 1)

            def spatial_gate(u, s, j):
                g = 2 * (s % 2) + j
                n = 2 * u + j
                act.wait_ge(aff2, 4 * n + 4)
                act.wait_ge(sq2_done, n + 1)
                flat = sp_buf[:, g].rearrange("p b w -> p (b w)")
                nc.scalar.activation(flat, flat, ACT.Sigmoid, scale=scale2[:, g:g + 1],
                                     bias=bias2[:, g:g + 1]).then_inc(sig2, 1)

            def body(t, q):
                a, sa = t + 1, (q + 1) % XS
                da = sa % 2
                b, sb_ = t - 1, (q - 1) % XS
                if real(b):
                    evacuate(b, sb_, 3)
                if real(a):
                    act.wait_ge(mean_mm, a + 1)
                    if later(a, 4):
                        act.wait_ge(final, 2 * (a - XS) + 2)
                    nc.scalar.activation(negm[:, sa], norm_ps[:, 0:2], ACT.Copy, scale=-1.0).then_inc(negm_done, 1)
                    act.wait_ge(negm_done, a + 1)
                    for j in range(2):
                        act.wait_ge(x_in[sa][j], 4 * RB * (a - sa) + 16 * RB)
                        if later(a, 1):
                            act.wait_ge(sq_done, 2 * a + j - 1)
                        nc.scalar.activation(junk[:, j], xt[:, sa, j].rearrange("p b w -> p (b w)"), ACT.Square,
                                             bias=negm[:, sa, j:j + 1],
                                             accum_out=ssq[:, da, j:j + 1]).then_inc(sq_done, 1)
                if real(b):
                    square2(b, sb_, 1)
                if real(t):
                    evacuate(t, q, 0)
                if real(a):
                    pos = pos_ps[:, 0:2 * (NB + W)].rearrange("p (j n) -> p j n", j=2)
                    act.wait_ge(pos_mm, a + 1)
                    act.wait_ge(rstd_done, a + 1)
                    for j in range(2):
                        nc.scalar.activation(gate_h[:, da, j], pos[:, j, 0:NB], ACT.Sigmoid,
                                             scale=rstd[:, sa, j:j + 1], bias=b_pos[:, 0:1]).then_inc(gates_done, 1)
                    if later(a, 2):
                        act.wait_ge(gp_dve, 2 * (a - 1))
                    for j in range(2):
                        nc.scalar.activation(gate_w[:, da, j], pos[:, j, NB:NB + W], ACT.Sigmoid,
                                             scale=rstd[:, sa, j:j + 1], bias=b_pos[:, 1:2]).then_inc(gates_done, 1)

                def gate_products(j):
                    if real(a):
                        act.wait_ge(ghr_done, a + 1)
                        act.wait_ge(gates_done, 4 * a + 4)
                        if later(a, 2):
                            act.wait_ge(conv_mm, 4 * (a - 2) + 4)
                        for i in range(ACT_BANDS):
                            ins = nc.scalar.activation(gated[:, da, j, i, 1:1 + W], gate_w[:, da, j], ACT.Copy,
                                                       scale=gate_hr[:, da, j, i:i + 1])
                        ins.then_inc(gp_act, 1)

                if real(b):
                    variance2(b, sb_, 1)
                gate_products(0)
                if real(t):
                    evacuate(t, q, 1)
                gate_products(1)
                if real(b):
                    spatial_gate(b, sb_, 1)
                if real(t):
                    square2(t, q, 0)
                if real(a):
                    act.wait_ge(cgn, 9 * a + 9)
                    if later(a, 2):
                        act.wait_ge(kfac_done, a - 1)
                    nc.scalar.activation(cgate[:, da], ch[:, 9], ACT.Sigmoid).then_inc(cgate_done, 1)
                if real(t):
                    evacuate(t, q, 2)
                    variance2(t, q, 0)
                    spatial_gate(t, q, 0)

            turns(act, body)

        @block.vector
        def _(dve):
            made = [0]

            def link(ins):
                made[0] += 1
                ins.then_inc(w_dve, 1)
                dve.wait_ge(w_dve, made[0])

            dve.wait_ge(w_in, 16 * W_LOADS)
            def expand(dst, rep, mask, parts=P):
                link(nc.vector.tensor_tensor(dst.rearrange("p (o r) -> p o r", r=RB),
                                             rep.unsqueeze(2).to_broadcast([parts, CG, RB]),
                                             mask.unsqueeze(1).to_broadcast([parts, CG, RB]), ALU.mult))

            for kw in range(KW):
                expand(W_conv[:, kw], wconv_rep[:, kw, 1], masks[:, 1])
                for i, kh in enumerate((0, 2)):
                    expand(w_part[:, i, kw], wconv_rep[:, kw, kh], masks[:, kh])
                    link(nc.vector.tensor_tensor(W_conv[:, kw], W_conv[:, kw], w_part[:, i, kw], ALU.add))
            expand(W_halo[:, :], whalo_in[:, :], hmask[:, :], HALO)
            expand(W_s1h[:, :], ws1_rep[:, :], masks[:, 1])
            expand(W_ph[:, :], wph_rep[:, :], masks[:, 1])
            expand(W_pw[:, :], wpw_rep[:, :], masks[:, 1])
            expand(W_gmp[:, :], wcc_rep[:, 1], masks[:, 1])
            for dst, rep in ((W_s1w, ws1_rep[:, :]), (W_gap, wcc_rep[:, 0])):
                link(nc.vector.tensor_scalar(dst[:, :].rearrange("p (o r) -> p o r", r=RB),
                                             rep.unsqueeze(2).to_broadcast([P, CG, RB]), 1.0 / RB, None, ALU.mult))
            link(nc.vector.tensor_scalar(M_chan[:, :], S_chan[:, :], 1.0 / PIX, None, ALU.mult))
            link(nc.vector.tensor_scalar(mask_pix[:, :], masks[:, 1], float(PIX), None, ALU.mult))
            dve.wait_ge(w_pe, 1)
            link(nc.vector.tensor_copy(W_rows[:, :], pos_ps[:, 0:P]))
            link(nc.vector.tensor_copy(W_cols[:, :], pos_ps[:, P:2 * P]))
            link(nc.vector.tensor_tensor(b_pos[:, :], pos_ps[:, 2 * P:2 * P + 2], vec[:, 4:6], ALU.add))
            for s in range(2):
                for col in (0, WP - 1):
                    link(nc.vector.memset(gated[:, s, :, :, col:col + 1], 0.0))

            def finish(u, s, j):
                g = 2 * (s % 2) + j
                n = 2 * u + j
                flat = sp_buf[:, g].rearrange("p b w -> p (b w)")
                xf = xt[:, s, j].rearrange("p b w -> p (b w)")
                dve.wait_ge(sig2, n + 1)
                nc.vector.scalar_tensor_tensor(flat, xf, negm[:, s, j:j + 1], flat, ALU.add, ALU.mult).then_inc(fin_a, 1)
                dve.wait_ge(fin_a, n + 1)
                dve.wait_ge(kfac_done, u + 1)
                nc.vector.scalar_tensor_tensor(flat, flat, kfac[:, s, j:j + 1], xf, ALU.mult, ALU.add).then_inc(final, 1)

            def body(t, q):
                a, sa = t + 1, (q + 1) % XS
                da = sa % 2
                b, sb_ = t - 1, (q - 1) % XS
                c, sc = t + 2, (q + 2) % XS
                dc = sc % 2
                if real(b):
                    finish(b, sb_, 0)
                if real(a):
                    dve.wait_ge(negm_done, a + 1)
                    if later(a, 2):
                        dve.wait_ge(pos_mm, a - 1)
                    for j in range(2):
                        nc.vector.tensor_scalar(sums_n[:, da, j, 0:NB], sums[:, da, j, 0:NB], 1.0 / W,
                                                negm[:, sa, j:j + 1], ALU.mult, ALU.add)
                        ins = nc.vector.tensor_scalar(sums_n[:, da, j, NB:], sums[:, da, j, NB:], 1.0 / NB,
                                                      negm[:, sa, j:j + 1], ALU.mult, ALU.add)
                    ins.then_inc(sn_done, 1)
                def row_sums(j):
                    if real(c):
                        if later(c, 2):
                            dve.wait_ge(sn_done, c - 1)
                        dve.wait_ge(x_in[sc][j], 4 * RB * (c - sc) + 16 * RB)
                        nc.vector.tensor_reduce(sums[:, dc, j, 0:NB], xt[:, sc, j], AX_X,
                                                ALU.add).then_inc(sums_done, 1)

                def column_sums(j):
                    if real(c):
                        nc.vector.tensor_reduce(sums[:, dc, j, NB:], xt[:, sc, j].rearrange("p b w -> p w b"), AX_X,
                                                ALU.add).then_inc(sums_done, 1)

                def modulate(j):
                    if real(a):
                        dve.wait_ge(gp_act, 2 * a + j + 1)
                        dve.wait_ge(gp_dve, 2 * a + j + 1)
                        nc.vector.scalar_tensor_tensor(gated[:, da, j, :, 1:1 + W], xt[:, sa, j],
                                                       negm[:, sa, j:j + 1], gated[:, da, j, :, 1:1 + W],
                                                       ALU.add, ALU.mult).then_inc(mod_done, 1)

                row_sums(0)
                if real(a):
                    dve.wait_ge(spread_mm, a + 1)
                    if real(b):
                        dve.wait_ge(negm2_done, 2 * b + 2)
                    if later(a, 2):
                        dve.wait_ge(cin, 3 * (a - 1))
                    nc.vector.tensor_reduce(gmx[:, da], gn2_ps[:, MAXIMA].rearrange("p (j r) -> p j r", j=2),
                                            AX_X, ALU.max).then_inc(gmx_done, 1)
                    dve.wait_ge(var_mm, a + 1)
                    if later(a, 2):
                        dve.wait_ge(rstd_done, a - 1)
                    nc.vector.tensor_scalar(var_e[:, da], norm_ps[:, 2:4], EPS, None, ALU.add).then_inc(var_done, 1)
                row_sums(1)
                if real(c):
                    dve.wait_ge(sums_done, 4 * c + 2)
                    if later(c, 2):
                        dve.wait_ge(cin, 3 * (c - 2) + 1)
                    nc.vector.tensor_reduce(tot[:, dc], sums[:, dc, :, 0:NB], AX_X, ALU.add).then_inc(tot_done, 1)
                if real(a):
                    dve.wait_ge(gates_done, 4 * a + 4)
                    dve.wait_ge(rstd_done, a + 1)
                    if later(a, 2):
                        dve.wait_ge(gp_act, 2 * (a - 1))
                    nc.vector.tensor_tensor(gate_hr[:, da], gate_h[:, da],
                                            rstd[:, sa].unsqueeze(2).to_broadcast([P, 2, NB]),
                                            ALU.mult).then_inc(ghr_done, 1)
                    dve.wait_ge(ghr_done, a + 1)
                    if later(a, 2):
                        dve.wait_ge(conv_mm, 4 * (a - 2) + 4)
                    for j in range(2):
                        nb = NB - ACT_BANDS
                        nc.vector.tensor_tensor(gated[:, da, j, ACT_BANDS:, 1:1 + W],
                                                gate_w[:, da, j].unsqueeze(1).to_broadcast([P, nb, W]),
                                                gate_hr[:, da, j, ACT_BANDS:].unsqueeze(2).to_broadcast([P, nb, W]),
                                                ALU.mult).then_inc(gp_dve, 1)
                column_sums(0)
                column_sums(1)
                if real(a):
                    dve.wait_ge(ch_mm, a + 1)
                    if later(a, 1):
                        dve.wait_ge(cgn, 9 * (a - 1) + 1)
                    nc.vector.tensor_tensor(ch[:, 0], cw_ps[:, 0:2], rstd[:, sa], ALU.mult).then_inc(ch_done, 1)
                if real(c):
                    if later(c, 1):
                        dve.wait_ge(mxx_done, c)
                    nc.vector.tensor_reduce(mx[:, dc], xt[:, sc].rearrange("p j b w -> p j (b w)"), AX_X,
                                            ALU.max).then_inc(mx_done, 1)
                    dve.wait_ge(mx_done, c + 1)
                    if later(c, 2):
                        dve.wait_ge(spread_mm, c - 1)
                    nc.vector.tensor_tensor(spread_in[:, dc, 2:].rearrange("p (j r) -> p j r", j=2), mx[:, dc].unsqueeze(2).to_broadcast([P, 2, RB]),
                                            mask_pix[:, :].unsqueeze(1).to_broadcast([P, 2, RB]),
                                            ALU.mult).then_inc(mxx_done, 1)
                modulate(0)
                modulate(1)
                if real(b):
                    finish(b, sb_, 1)

            turns(dve, body)

        @block.tensor
        def _(pe):
            pe.wait_ge(w_dve, 24)
            nc.tensor.matmul(pos_ps[:, 0:P], W_s1h[:, :], W_ph[:, :], start=True, stop=True)
            nc.tensor.matmul(pos_ps[:, P:2 * P], W_s1w[:, :], W_pw[:, :], start=True, stop=True)
            nc.tensor.matmul(pos_ps[:, 2 * P:2 * P + 1], W_ph[:, :], V["b_s1"], start=True, stop=True)
            nc.tensor.matmul(pos_ps[:, 2 * P + 1:2 * P + 2], W_pw[:, :], V["b_s1"], start=True,
                             stop=True).then_inc(w_pe, 1)
            pe.wait_ge(w_dve, 27)
            pe.wait_ge(w_pool, 6)

            pos = pos_ps[:, 0:2 * (NB + W)].rearrange("p (j n) -> p j n", j=2)

            def mm(ps, lhsT, rhs, start=True, stop=True):
                return nc.tensor.matmul(ps, lhsT, rhs, start=start, stop=stop)

            def body(t, q):
                a, sa = t + 1, (q + 1) % XS
                da = sa % 2
                b, sb_ = t - 1, (q - 1) % XS

                def mean():
                    if real(a):
                        pe.wait_ge(tot_done, a + 1)
                        if later(a, 1):
                            pe.wait_ge(var_done, a)
                        mm(norm_ps[:, 0:2], M_all[:, :], tot[:, da]).then_inc(mean_mm, 1)

                def spread():
                    if real(b) or real(a):
                        lo = 0 if real(b) else 2
                        hi = 2 + 2 * RB if real(a) else 2
                        if real(b):
                            pe.wait_ge(evac, 4 * b + 4)
                            pe.wait_ge(var2_done, 2 * b + 1)
                        if real(a):
                            pe.wait_ge(mxx_done, a + 1)
                            if later(a, 1):
                                pe.wait_ge(gmx_done, a)
                        mm(gn2_ps[:, lo:hi], M_chan[:, :], spread_in[:, da, lo:hi]).then_inc(spread_mm, 1)

                def mean2_first():
                    if real(t):
                        pe.wait_ge(evac, 4 * t + 2)
                        if not real(b):
                            pe.wait_ge(gmx_done, a + 1)
                        else:
                            pe.wait_ge(var2_done, 2 * t)
                        mm(gn2_ps[:, 0:2], M_chan[:, :], ssum2_first[:, q % 2]).then_inc(mean2_mm, 1)

                def var2(u, s, j):
                    if real(u):
                        g = 2 * (s % 2) + j
                        n = 2 * u + j
                        pe.wait_ge(sq2_done, n + 1)
                        pe.wait_ge(negm2_done, n + 1)
                        if j == 1 and real(a):
                            pe.wait_ge(gmx_done, a + 1)
                        mm(gn2_ps[:, VAR2], M_chan[:, :], ssq2[:, g:g + 1]).then_inc(var2_mm, 1)

                def variance():
                    if real(a):
                        pe.wait_ge(sq_done, 2 * a + 2)
                        pe.wait_ge(negm_done, a + 1)
                        mm(norm_ps[:, 2:4], M_all[:, :], ssq[:, da]).then_inc(var_mm, 1)

                def positions():
                    if real(a):
                        pe.wait_ge(sn_done, a + 1)
                        if later(a, 1):
                            pe.wait_ge(gates_done, 4 * a)
                        mm(pos[:, :, 0:NB], W_rows[:, :], sums_n[:, da, :, 0:NB])
                        mm(pos[:, :, NB:NB + W], W_cols[:, :], sums_n[:, da, :, NB:]).then_inc(pos_mm, 1)

                def channel():
                    if real(a):
                        pe.wait_ge(cin, 3 * a + 3)
                        if later(a, 1):
                            pe.wait_ge(ch_done, a)
                        mm(cw_ps[:, 0:2], W_gap[:, :], gap_n[:, da], stop=False)
                        mm(cw_ps[:, 0:2], W_gmp[:, :], gmx_n[:, da], start=False).then_inc(ch_mm, 1)

                def conv(h, first, last):
                    if not real(t):
                        return
                    j, k = h // 2, h % 2
                    d = q % 2
                    if first == 0:
                        pe.wait_ge(mod_done, 2 * t + j + 1)
                        if later(4 * t + h, 2):
                            pe.wait_ge(evac, 4 * t + h - 1)
                    for i in range(first, last):
                        w, bank = i // 2, i % 2
                        band = (2 * k + bank) * BB
                        o = conv_ps[:, h % 2, bank * BB:(bank + 1) * BB]
                        if w < KW:
                            mm(o, W_conv[:, w], gated[:, d, j, band:band + BB, w:w + W],
                               start=w == 0, stop=False)
                        else:
                            if bank == 0:
                                pe.wait_ge(halo_in[d][j], 16 * (t - d) + 32)
                            rows = halo[:, d, j].rearrange("p (b w) -> p b w", w=WP)
                            ins = mm(o, W_halo[:, :], rows[:, band:band + BB, 0:W], start=False)
                    if last == 8:
                        ins.then_inc(conv_mm, 1)

                mean()
                conv(0, 0, 2)
                spread()
                conv(0, 2, 7)
                variance()
                conv(0, 7, 8)
                positions()
                conv(1, 0, 1)
                var2(b, sb_, 1)
                conv(1, 1, 7)
                channel()
                conv(1, 7, 8)
                conv(2, 0, 3)
                mean2_first()
                conv(2, 3, 8)
                conv(3, 0, 4)
                var2(t, q, 0)
                conv(3, 4, 8)

            turns(pe, body)


_VECS = ["b_cc", "gn1_w", "gn1_b", "b_s1", "b_ph", "b_pw", "b_s3", "gn2_w", "gn2_b"]


def kernel(**inputs):
    import numpy as np
    import concourse.bacc as bacc
    from concourse.bass_utils import run_bass_kernel_spmd

    def get(name):
        return np.asarray(inputs["L0_conv_" + name])

    r = np.arange(P) % RB
    o = np.arange(RB)
    same_channel = (np.arange(P)[:, None] // RB == np.arange(P)[None, :] // RB).astype(np.float32)
    row_masks = np.stack([o[None, :] == (r[:, None] + 1 - kh) for kh in range(3)], 1).astype(np.float32)
    halo_mask = np.zeros((HALO, RB), np.float32)
    halo_mask[:HALO // 2, 0] = 1
    halo_mask[HALO // 2:, RB - 1] = 1
    wconv = get("w_s3").transpose(1, 3, 2, 0).reshape(CG, KW * 3 * CG)
    arrays = {
        "x": np.asarray(inputs["x"]),
        "by_channel": np.concatenate([get("w_cc").reshape(CG, 2, CG).transpose(2, 1, 0).reshape(CG, 2 * CG),
                                      wconv, get("w_s1"), get("w_ph").T, get("w_pw").T,
                                      np.stack([get(n) for n in _VECS], 1)], 1),
        "wconv": wconv,
        "same_channel": same_channel,
        "row_masks": row_masks.reshape(P, 3 * RB),
        "halo_mask": halo_mask,
    }
    arrays = {f"in_{n}": np.ascontiguousarray(a) for n, a in arrays.items()}
    nc = bacc.Bacc("TRN2", target_bir_lowering=False, num_devices=1)
    t = {n[3:]: nc.dram_tensor(n, a.shape, mybir.dt.from_np(a.dtype), kind="ExternalInput").ap()
         for n, a in arrays.items()}
    out = nc.dram_tensor("out_0", (N, C, HT, W), F32, kind="ExternalOutput").ap()
    conv_attention(nc, t["x"], t["by_channel"], t["wconv"],
                   t["same_channel"], t["row_masks"], t["halo_mask"], out)
    res = run_bass_kernel_spmd(nc, [arrays], core_ids=[0])
    return res.results[0]["out_0"]
```
